# Optimizing a Trainium2 kernel written in Bass

```python
import numpy as np
import jax
import jax.numpy as jnp

def _softmax(x, axis=-1):
    return jax.nn.softmax(x, axis=axis)

def _gelu(x):
    return jax.nn.gelu(x, approximate=True)

def _silu(x):
    return jax.nn.silu(x)

def _sigmoid(x):
    return jax.nn.sigmoid(x)

def _layernorm(x, axis=-1, eps=1e-05):
    m = jnp.mean(x, axis=axis, keepdims=True)
    v = jnp.var(x, axis=axis, keepdims=True)
    return (x - m) / jnp.sqrt(v + eps)

def _scatter_add(tgt, idx, src, axis=0):
    return tgt.at[idx].add(src)

def _segment_sum(src, seg, n):
    return jax.ops.segment_sum(src, seg, n)
kernel_name = 'mk_macaron_d1_jaxref_r8_67fd59'

def setup_inputs(seed: int=0):
    np.random.seed(seed)
    _w = jnp.asarray

    def _L0_attn_setup():
        import jax, jax.numpy as jnp
        import numpy as np
        K_FACTOR = 0.5
        key = jax.random.key(seed)
        k1, k2, k3, k4 = jax.random.split(key, 4)
        B, S, H, I = (1, 256, 512, 1376)
        x = jax.random.normal(k1, (B, S, H), dtype=jnp.float32)
        w_gate = jax.random.normal(k2, (I, H), dtype=jnp.float32) * 0.02
        w_up = jax.random.normal(k3, (I, H), dtype=jnp.float32) * 0.02
        w_down = jax.random.normal(k4, (H, I), dtype=jnp.float32) * 0.02
        return {'x': x, 'w_gate': w_gate, 'w_up': w_up, 'w_down': w_down}
    _L0_attn_in = _L0_attn_setup()

    def _L0_ffn_setup():
        import jax, jax.numpy as jnp
        import numpy as np
        BATCH, SEQ, D = (2, 256, 512)
        K, TOPK, RANK = (64, 16, 16)
        ALPHA = 32.0
        SCALING = ALPHA / RANK
        key = jax.random.key(seed)
        k1, k2, k3, k4 = jax.random.split(key, 4)
        x = jax.random.normal(k1, (BATCH, SEQ, D), dtype=jnp.float32)
        A = jax.random.normal(k2, (K, RANK, D), dtype=jnp.float32) * 0.02
        B = jax.random.normal(k3, (K, D, RANK), dtype=jnp.float32) * 0.02
        Wr = jax.random.normal(k4, (K, D), dtype=jnp.float32) * 0.02
        return {'x': x, 'A': A, 'B': B, 'Wr': Wr}
    _L0_ffn_in = _L0_ffn_setup()
    _d = {'L0_attn_x': _L0_attn_in['x'], 'L0_attn_w_gate': _L0_attn_in['w_gate'], 'L0_attn_w_up': _L0_attn_in['w_up'], 'L0_attn_w_down': _L0_attn_in['w_down'], 'L0_ffn_A': _L0_ffn_in['A'], 'L0_ffn_B': _L0_ffn_in['B'], 'L0_ffn_Wr': _L0_ffn_in['Wr']}
    _x0 = _d['L0_attn_x']
    _d['L0_attn_x'] = jax.random.normal(jax.random.fold_in(jax.random.key(seed), 1), (8, 256, 512), dtype=_x0.dtype)
    del _x0
    return _d

def reference(L0_attn_x, L0_attn_w_gate, L0_attn_w_up, L0_attn_w_down, L0_ffn_A, L0_ffn_B, L0_ffn_Wr):

    def _L0_attn_ref(x, w_gate, w_up, w_down):
        import jax, jax.numpy as jnp
        import numpy as np
        K_FACTOR = 0.5
        s = jax.nn.silu(jnp.einsum('bsh,ih->bsi', x, w_gate))
        B, S, I = s.shape
        k = int(K_FACTOR * I)
        _, idx = jax.lax.top_k(-jnp.abs(s), k)
        flat = s.reshape(B * S, I)
        rows = jnp.arange(B * S)[:, None]
        flat = flat.at[rows, idx.reshape(B * S, k)].set(0.0)
        s = flat.reshape(B, S, I)
        s = s * jnp.einsum('bsh,ih->bsi', x, w_up)
        return jnp.einsum('bsi,hi->bsh', s, w_down)

    def _L0_ffn_ref(x, A, B, Wr):
        import jax, jax.numpy as jnp
        import numpy as np
        BATCH, SEQ, D = (2, 256, 512)
        K, TOPK, RANK = (64, 16, 16)
        ALPHA = 32.0
        SCALING = ALPHA / RANK
        prefix = x.shape[:-1]
        xf = x.reshape(-1, x.shape[-1])
        N = xf.shape[0]
        scores = xf @ Wr.T
        top_vals, top_idx = jax.lax.top_k(scores, TOPK)
        gates = jax.nn.softmax(top_vals, axis=-1)
        G = jnp.zeros((N, K), xf.dtype).at[jnp.arange(N)[:, None], top_idx].set(gates)
        h = jnp.einsum('nd,krd->nkr', xf, A)
        out = jnp.einsum('nkr,kdr->nd', h * G[:, :, None], B)
        return (out * SCALING).reshape(*prefix, -1)
    x = L0_attn_x
    x = x + 0.5 * _L0_ffn_ref(_layernorm(x, axis=-1), L0_ffn_A, L0_ffn_B, L0_ffn_Wr)
    x = x + _L0_attn_ref(_layernorm(x, axis=-1), L0_attn_w_gate, L0_attn_w_up, L0_attn_w_down)
    x = x + 0.5 * _L0_ffn_ref(_layernorm(x, axis=-1), L0_ffn_A, L0_ffn_B, L0_ffn_Wr)
    return x

_drawn_inputs = setup_inputs


def setup_inputs(seed=0):
    import zlib

    import numpy as np

    out = dict(_drawn_inputs(seed))
    spreads = {}
    factors = {'L0_ffn_A': 2.862, 'L0_ffn_B': 2.707, 'L0_ffn_Wr': 3.135}
    for name, (base, spread) in spreads.items():
        noise = np.random.default_rng([zlib.crc32(name.encode()), seed]).standard_normal(out[name].shape)
        drawn = base * np.exp(spread * noise) if base else spread * noise
        out[name] = jnp.asarray(drawn.astype(out[name].dtype))
    for name, factor in factors.items():
        out[name] = (out[name] * factor).astype(out[name].dtype)
    return out
```

```python
from contextlib import ExitStack

import concourse.bass as bass
from concourse import mybir

ALU = mybir.AluOpType
ACT = mybir.ActivationFunctionType
AX = mybir.AxisListType
F32 = mybir.dt.float32
F16 = mybir.dt.float16
BF16 = mybir.dt.bfloat16
I32 = mybir.dt.int32

P = 128
BANK = 512
EPS = 1e-5
TOPK = 16
NEG = -3.0e38
ROUNDS = 7
DAMP = (1.0, 0.9, 0.6, 0.5, 0.4, 0.4)
GUESS = 5.7715e-4
SPACING = 8.95e-7


class Matrix:

    def __init__(self, name, chunks, width, per_piece, last_rows, stage, at, bank):
        self.name, self.chunks, self.width = name, chunks, width
        self.pieces = []
        c = 0
        while c < chunks:
            if last_rows < P and c == chunks - 1:
                self.pieces.append((c, 1, last_rows))
                c += 1
                continue
            n = min(per_piece, (chunks - 1 if last_rows < P else chunks) - c)
            self.pieces.append((c, n, P))
            c += n
        self.stage, self.at, self.bank = stage, at, bank


class Chain:

    def __init__(self, engine, sem):
        self.engine, self.sem, self.base, self.count = engine, sem, 0, 0

    def __call__(self, instruction, wait=None):
        instruction.then_inc(self.sem, 1)
        self.count += 1
        if wait is None:
            self.engine.wait_ge(self.sem, self.base + self.count)
        else:
            wait(self.engine, self.sem, self.base + self.count)


def build(nc, x, w_r, w_a, w_b, w_g, w_u, w_d, out):
    N, D = x.shape
    KE, KR, I = w_r.shape[1], w_a.shape[1], w_g.shape[1]
    RANK = KR // KE
    NT = N // P
    DC, RC, IC = D // P, KR // P, -(-I // P)
    IPAD = IC * P
    LAST = I - (IC - 1) * P
    ZEROED = I // 2
    assert 2 * ZEROED == I and D == BANK and KR == 2 * BANK
    SQRT_D_BITS = 10
    XS = float(2 ** SQRT_D_BITS)
    GATE_S = 2.0 ** -15
    VAL_S = 2.0 ** -45
    LOOP_FROM, LOOP_TO = 4, NT - 2
    assert (LOOP_TO - LOOP_FROM) % 2 == 0

    MR = Matrix("r", DC, KE, DC, P, 0, 4 * KR, 7)
    MA = Matrix("a", DC, KR, 1, P, 0, 0, 5)
    MB = Matrix("b", RC, D, 2, P, 1, 0, 1)
    MG = Matrix("g", DC, I, 1, P, 0, 0, 2)
    MU = Matrix("u", DC, I, 1, P, 1, 0, 5)
    MD = Matrix("d", IC, D, 2, LAST, 0, 0, 1)
    MATS = [MR, MA, MB, MG, MU, MD]
    dram = {"r": w_r, "a": w_a, "b": w_b, "g": w_g, "u": w_u, "d": w_d}

    with ExitStack() as ctx:
        def sb(name, shape, dt):
            return ctx.enter_context(nc.sbuf_tensor(name, shape, dt))

        def sem(name):
            return ctx.enter_context(nc.semaphore(name))

        ps = ctx.enter_context(nc.psum_tensor("ps", [P, 8 * BANK], F32))

        def bank(b, n=BANK, lo=0):
            return ps[:, b * BANK + lo:b * BANK + lo + n]

        hi = {m.name: sb(f"w_{m.name}_hi", [P, m.chunks, m.width], F16) for m in MATS}
        lo = {m.name: sb(f"w_{m.name}_lo", [P, m.chunks, m.width], F16) for m in MATS}
        stages = [sb("stage0", [P, IC * BANK], F32), sb("stage1", [P, IC * BANK], F32)]
        val = [stages[1][:, IPAD * b:IPAD * (b + 1)] for b in range(2)]
        cand = stages[1][:, 2 * IPAD:2 * IPAD + I]
        mag = [sb(f"mag{b}", [P, I], F32) for b in range(2)]
        gate = sb("gate", [P, I], F32)
        keep = sb("keep", [P, I], F16)
        signs = sb("signs", [P, I], BF16)
        squares = [signs[:, :], keep[:, :].bitcast(BF16)]
        xin = [sb(f"xin{b}", [P, D], F32) for b in range(2)]
        x1 = [sb(f"x1_{b}", [P, D], F32) for b in range(2)]
        x2 = sb("x2", [P, D], F32)
        y = [sb(f"y{b}", [P, D], F32) for b in range(2)]
        normed = {j: sb(f"normed{j}", [P, D], F32) for j in (1, 2, 3)}
        xt_hi = {j: sb(f"xt_hi{j}", [P, DC, P], F16) for j in (1, 2, 3)}
        xt_lo = {j: sb(f"xt_lo{j}", [P, DC, P], F16) for j in (1, 2, 3)}
        routed = sb("routed", [P, KR], F32)
        pt_hi = sb("pt_hi", [P, RC, P], F16)
        pt_lo = sb("pt_lo", [P, RC, P], F16)
        vt_hi = sb("vt_hi", [P, IC, P], F16)
        vt_lo = sb("vt_lo", [P, IC, P], F16)
        ident = sb("ident", [P, P], F32)
        ones = sb("ones", [P, P], BF16)
        scores = sb("scores", [P, KE], F32)
        work1 = sb("work1", [P, KE], F32)
        work2 = sb("work2", [P, KE], F32)
        expd = sb("expd", [P, KE], F32)
        chosen = sb("chosen", [P, KE], F32)
        weight = sb("weight", [P, KE], F32)
        flags = sb("flags", [P, 32], F32)
        flags_t = sb("flags_t", [P, 32], F32)
        small = sb("small", [P, 64], F32)
        ints = sb("ints", [P, 16], I32)
        stats = {j: sb(f"stats{j}", [P, 6], F32) for j in (1, 2, 3)}
        mv = {j: sb(f"mv{j}", [P, 2], F32) for j in (1, 2, 3)}

        cols = {}

        def col(name, n=1, t=small):
            if name not in cols:
                cols[name] = cols.get("#", 0)
                cols["#"] = cols[name] + n
                assert cols["#"] <= 64
            return t[:, cols[name]:cols[name] + n]

        top_a, top_b, cand8, evens = (col(n, 8) for n in ("top_a", "top_b", "cand8", "evens"))
        neg_max, total, inv_total = col("neg_max"), col("total"), col("inv_total")
        mag_sum, step, thr, bal, off, far, move = (
            col(n) for n in ("mag_sum", "step", "thr", "bal", "off", "far", "move"))
        kth, above = col("kth"), col("above")
        unscale_r, unscale_f, unscale_g, unscale_m = (
            col(n) for n in ("unscale_r", "unscale_f", "unscale_g", "unscale_m"))
        scale = {m.name: col("scale_" + m.name) for m in MATS}
        half_exp = {m.name: col("half_exp_" + m.name) for m in MATS}
        norm2 = col("norm2")
        exp_sum = col("exp_sum")
        rvar = {j: sb(f"rvar{j}", [P, 2], F32) for j in (1, 2, 3)}
        neg_half = sb("neg_half", [P, 1], F32)
        flagged = ints[:, 8:9]

        x_loaded = [sem(f"x_loaded{b}") for b in range(2)]
        stored = [sem(f"stored{b}") for b in range(2)]
        w_loaded = {m.name: [sem(f"w_{m.name}_loaded{n}") for n in range(len(m.pieces))]
                    for m in MATS}
        const_made = sem("const_made")
        squared, norm_summed, scale_made = sem("squared"), sem("norm_summed"), sem("scale_made")
        w_hi_made, w_lo_made = sem("w_hi_made"), sem("w_lo_made")
        var_ready = {j: sem(f"var_ready{j}") for j in (1, 2, 3)}
        rstd_half = sem("rstd_half")
        rstd_ready = {j: sem(f"rstd_ready{j}") for j in (1, 2, 3)}
        normed_ready = {j: sem(f"normed_ready{j}") for j in (1, 2, 3)}
        xt_turned = {j: sem(f"xt_turned{j}") for j in (1, 2, 3)}
        xt_hi_ready = {j: sem(f"xt_hi_ready{j}") for j in (1, 2, 3)}
        xt_lo_ready = {j: sem(f"xt_lo_ready{j}") for j in (1, 2, 3)}
        scores_done = {j: sem(f"scores_done{j}") for j in (1, 3)}
        experts_done = {j: sem(f"experts_done{j}") for j in (1, 3)}
        max_ready = {j: sem(f"max_ready{j}") for j in (1, 3)}
        exp_ready = {j: sem(f"exp_ready{j}") for j in (1, 3)}
        routed_ready = {j: sem(f"routed_ready{j}") for j in (1, 3)}
        pt_turned = {j: sem(f"pt_turned{j}") for j in (1, 3)}
        pt_hi_ready = {j: sem(f"pt_hi_ready{j}") for j in (1, 3)}
        pt_lo_ready = {j: sem(f"pt_lo_ready{j}") for j in (1, 3)}
        ffn1_done, down_done, ffn3_done = sem("ffn1_done"), sem("down_done"), sem("ffn3_done")
        x1_ready, out_read = sem("x1_ready"), sem("out_read")
        gate_done, up_done = sem("gate_done"), sem("up_done")
        tanh_ready, gate_ready, mag_ready = sem("tanh_ready"), sem("gate_ready"), sem("mag_ready")
        thr_ready, counted = sem("thr_ready"), sem("counted")
        val_ready, kept_ready = sem("val_ready"), sem("kept_ready")
        vt_turned, vt_hi_ready, vt_lo_ready = (
            sem("vt_turned"), sem("vt_hi_ready"), sem("vt_lo_ready"))
        dve_chain = sem("dve_chain")

        def pieces_before(m):
            return sum(len(k.pieces) for k in MATS[:MATS.index(m)])

        def stage(m, c, n, rows):
            a = stages[m.stage][0:rows, m.at + c * m.width:m.at + (c + n) * m.width]
            return a.rearrange("p (c w) -> p c w", c=n)

        def nth(t, parity):
            return 8 * (t - parity) + 16

        def wait_apart(engine, semaphore, value):
            if not isinstance(value, int):
                value = engine.to_reg(value)
                engine.wait_ge(const_made, 4)
            engine.wait_ge(semaphore, value)

        def loop_steps(engine, emit, chain=None, per_step=0):
            for i in range(LOOP_FROM):
                emit(i, i % 2, i)
            if chain is not None:
                chain.base, before, chain.count = chain.count, chain.count, 0
            with engine.Fori(LOOP_FROM, LOOP_TO, 2) as i:
                if chain is not None:
                    chain.base = i * per_step + (before - LOOP_FROM * per_step)
                emit(i, 0, LOOP_FROM)
                emit(i + 1, 1, LOOP_FROM)
                if chain is not None:
                    assert chain.count == 2 * per_step, chain.count
            if chain is not None:
                chain.base, chain.count = before + (LOOP_TO - LOOP_FROM) * per_step, 0
            for i in range(LOOP_TO, NT + 2):
                emit(i, i % 2, i)

        def parts(like):
            return like < NT, like + 1 < NT, 1 <= like <= NT, like >= 2

        block = ctx.enter_context(nc.Block())

        @block.sync
        def _(sp):
            def load_x(i, b, like):
                if like >= 2:
                    sp.wait_ge(x1_ready, i - 1)
                sp.dma_start(xin[b][:, :], x[bass.ds(i * P, P), :]).then_inc(x_loaded[b], 16)

            def load_w(m, after=None):
                if after is not None:
                    sp.wait_ge(w_hi_made, pieces_before(after) + len(after.pieces))
                    sp.wait_ge(w_lo_made, pieces_before(after) + len(after.pieces))
                for n, (c, k, rows) in enumerate(m.pieces):
                    src = dram[m.name][c * P:c * P + (k - 1) * P + rows, :]
                    sp.dma_start(stage(m, c, k, rows), src.rearrange("(c p) w -> p c w", c=k)
                                 ).then_inc(w_loaded[m.name][n], 16)

            def emit(i, b, like):
                cur, nxt, med, mid = parts(like)
                if like == 0:
                    load_w(MG, MA)
                    load_w(MU, MB)
                    load_w(MD, MG)
                if nxt and like >= 1:
                    load_x(i + 1, 1 - b, like + 1)
                if mid:
                    sp.wait_ge(out_read, 2 * i)
                    sp.dma_start(out[bass.ds((i - 2) * P, P), :], y[b][:, :]).then_inc(stored[b], 16)

            load_x(0, 0, 0)
            load_w(MR)
            load_w(MA)
            load_x(1, 1, 1)
            load_w(MB)
            loop_steps(sp, emit)
            for b in range(2):
                sp.wait_ge(stored[b], nth(NT - 2 + b, b))

        @block.gpsimd
        def _(pool):
            pool.memset(ones[:, :], 1.0).then_inc(const_made, 1)
            pool.memset(neg_half[:, :], -0.5).then_inc(const_made, 1)
            pool.memset(ident[:, :], 0.0).then_inc(const_made, 1)
            pool.wait_ge(const_made, 3)
            pool.affine_select(out=ident[:, :], in_=ident[:, :], compare_op=ALU.not_equal, fill=1.0,
                               base=0, pattern=[[-1, P]], channel_multiplier=1
                               ).then_inc(const_made, 1)

            def rstd(j, t, turn):
                wait_apart(pool, var_ready[j], t + 1)
                pool.tensor_scalar(rvar[j][:, 0:1], mv[j][:, 1:2], EPS, XS ** -2, ALU.add, ALU.mult
                                   ).then_inc(rstd_half, 1)
                pool.wait_ge(rstd_half, turn)
                pool.tensor_tensor(rvar[j][:, 1:2], rvar[j][:, 0:1], neg_half[:, :], ALU.pow
                                   ).then_inc(rstd_ready[j], 1)

            def emit(i, b, like):
                cur, nxt, med, mid = parts(like)
                if like < 2:
                    before = 1 + 2 * i
                elif like < NT:
                    before = 3 * i - 1
                else:
                    before = 2 * NT - 2 + i
                n = 0
                if mid:
                    n += 1
                    rstd(3, i - 2, before + n)
                if cur:
                    n += 1
                    rstd(2, i, before + n)
                if nxt:
                    n += 1
                    rstd(1, i + 1, before + n)

            rstd(1, 0, 1)
            loop_steps(pool, emit)

        @block.tensor
        def _(pe):
            def three(dst, m, k, cols, x_hi, x_lo, start, stop):
                w_hi, w_lo = hi[m.name][:, k, cols], lo[m.name][:, k, cols]
                pe.matmul(dst, x_hi, w_hi, start=start, stop=False)
                pe.matmul(dst, x_lo, w_hi, start=False, stop=False)
                return pe.matmul(dst, x_hi, w_lo, start=False, stop=stop)

            def norms(m):
                for n, (c, k, rows) in enumerate(m.pieces):
                    turn = pieces_before(m) + n
                    pe.wait_ge(squared, turn + 1)
                    sq = squares[turn % 2]
                    for q in range(k):
                        for o in range(0, m.width, BANK):
                            w = min(BANK, m.width - o)
                            mm = pe.matmul(bank(m.bank + o // BANK, w), ones[0:rows, :],
                                           sq[0:rows, q * m.width + o:q * m.width + o + w],
                                           start=c + q == 0, stop=c + q == m.chunks - 1)
                    mm.then_inc(norm_summed, 1)

            def split_done(m):
                pe.wait_ge(w_hi_made, pieces_before(m) + len(m.pieces))
                pe.wait_ge(w_lo_made, pieces_before(m) + len(m.pieces))

            def turn_x(j, t):
                pe.wait_ge(normed_ready[j], t + 1)
                for c in range(DC):
                    mm = pe.transpose(bank(0, P, c * P), normed[j][:, c * P:(c + 1) * P],
                                      ident[:, :])
                mm.then_inc(xt_turned[j], 1)

            def turn_p(j, t, first):
                pe.wait_ge(routed_ready[j], t + 1)
                for c in range(RC):
                    mm = pe.transpose(bank(first + c // 4, P, (c % 4) * P),
                                      routed[:, c * P:(c + 1) * P], ident[:, :])
                    if c % 4 == 3:
                        mm.then_inc(pt_turned[j], 1)

            def turn_v(i, b, like):
                pe.wait_ge(kept_ready, i - 1)
                if like <= NT:
                    pe.wait_ge(gate_ready, i)
                for c in range(IC):
                    mm = pe.transpose(bank(2 + c // 4, P, (c % 4) * P),
                                      val[b][:, c * P:(c + 1) * P], ident[:, :])
                    if c % 4 == 3 or c == IC - 1:
                        mm.then_inc(vt_turned, 1)

            def wait_xt(j, t):
                pe.wait_ge(xt_hi_ready[j], t + 1)
                pe.wait_ge(xt_lo_ready[j], t + 1)

            def experts(j, hook=None):
                for k in range(DC):
                    mm = three(bank(7, KE), MR, k, slice(0, KE), xt_hi[j][:, k, :],
                               xt_lo[j][:, k, :], k == 0, k == DC - 1)
                mm.then_inc(scores_done[j], 1)
                for o in range(2):
                    for k in range(DC):
                        if hook is not None and o == 1 and k == 2:
                            hook()
                        mm = three(bank(5 + o), MA, k, slice(o * BANK, (o + 1) * BANK),
                                   xt_hi[j][:, k, :], xt_lo[j][:, k, :], k == 0, k == DC - 1)
                mm.then_inc(experts_done[j], 1)

            def combine(j, t, dst, done, hook=None):
                for c in range(RC):
                    if c % 4 == 0:
                        pe.wait_ge(pt_hi_ready[j], 2 * t + c // 4 + 1)
                        pe.wait_ge(pt_lo_ready[j], 2 * t + c // 4 + 1)
                    if hook is not None and c == 6:
                        hook()
                    mm = three(dst, MB, c, slice(0, D), pt_hi[:, c, :], pt_lo[:, c, :],
                               c == 0, c == RC - 1)
                mm.then_inc(done, 1)

            def wide(m, first, hook=None):
                for o in range(0, I, BANK):
                    w = min(BANK, I - o)
                    if hook is not None and o == 2 * BANK:
                        hook()
                    for k in range(DC):
                        mm = three(bank(first + o // BANK, w), m, k, slice(o, o + w),
                                   xt_hi[2][:, k, :], xt_lo[2][:, k, :], k == 0, k == DC - 1)
                return mm

            def down(i, hook):
                for c in range(IC):
                    if c % 4 == 0:
                        pe.wait_ge(vt_hi_ready, 3 * (i - 2) + c // 4 + 1)
                        pe.wait_ge(vt_lo_ready, 3 * (i - 2) + c // 4 + 1)
                    if c == 0:
                        pe.wait_ge(out_read, 2 * i - 2)
                    if c == 8:
                        hook()
                    mm = three(bank(1), MD, c, slice(0, D), vt_hi[:, c, :], vt_lo[:, c, :],
                               c == 0, c == IC - 1)
                mm.then_inc(down_done, 1)

            def emit(i, b, like):
                cur, nxt, med, mid = parts(like)
                if mid:
                    turn_v(i, b, like)
                if cur:
                    wait_xt(1, i)
                    if like >= 1:
                        pe.wait_ge(val_ready, i)
                    experts(1)
                if mid:
                    down(i, (lambda: turn_p(1, i, 5)) if cur else (lambda: None))
                elif cur:
                    turn_p(1, i, 5)
                if like == 0:
                    norms(MB)
                    split_done(MB)
                if cur:
                    if like >= 1:
                        pe.wait_ge(gate_ready, i)
                    combine(1, i, bank(4), ffn1_done,
                            (lambda: turn_x(3, i - 2)) if mid else None)
                elif mid:
                    turn_x(3, i - 2)
                if mid:
                    wait_xt(3, i - 2)
                    experts(3, (lambda: turn_x(2, i)) if cur else None)
                elif cur:
                    turn_x(2, i)
                if like == 0:
                    norms(MG)
                    split_done(MG)
                if cur:
                    wait_xt(2, i)
                    wide(MG, 2).then_inc(gate_done, 1)
                    if like == 0:
                        norms(MU)
                        split_done(MU)
                    if mid:
                        pe.wait_ge(routed_ready[3], i - 1)

                    def turn_last():
                        pe.wait_ge(gate_ready, i + 1)
                        turn_p(3, i - 2, 2)

                    wide(MU, 5, turn_last if mid else None).then_inc(up_done, 1)
                elif mid:
                    turn_p(3, i - 2, 2)
                if nxt:
                    turn_x(1, i + 1)
                if like == 0:
                    norms(MD)
                    split_done(MD)
                if mid:
                    pe.wait_ge(out_read, 2 * i - 1)
                    combine(3, i - 2, bank(1), ffn3_done)

            pe.wait_ge(const_made, 4)
            norms(MR)
            norms(MA)
            turn_x(1, 0)
            split_done(MR)
            split_done(MA)
            loop_steps(pe, emit)

        @block.scalar
        def _(act):
            def square(m):
                for n, (c, k, rows) in enumerate(m.pieces):
                    turn = pieces_before(m) + n
                    act.wait_ge(w_loaded[m.name][n], 16)
                    if turn >= 2:
                        act.wait_ge(norm_summed, turn - 1)
                    act.activation(
                        squares[turn % 2][0:rows, 0:k * m.width].rearrange("p (c w) -> p c w", c=k),
                        stage(m, c, k, rows), ACT.Square).then_inc(squared, 1)

            def split_hi(m):
                act.wait_ge(scale_made, MATS.index(m) + 1)
                for c, k, rows in m.pieces:
                    act.activation(hi[m.name][0:rows, c:c + k, :], stage(m, c, k, rows), ACT.Copy,
                                   scale=scale[m.name][0:rows, :]).then_inc(w_hi_made, 1)

            def xt_to_hi(j, t):
                act.wait_ge(xt_turned[j], t + 1)
                act.activation(xt_hi[j][:, :, :], bank(0).rearrange("p (c t) -> p c t", c=DC),
                               ACT.Copy).then_inc(xt_hi_ready[j], 1)

            def pt_to_hi(j, t, first):
                for h in range(2):
                    act.wait_ge(pt_turned[j], 2 * t + h + 1)
                    act.activation(pt_hi[:, 4 * h:4 * h + 4, :],
                                   bank(first + h).rearrange("p (c t) -> p c t", c=4),
                                   ACT.Copy).then_inc(pt_hi_ready[j], 1)

            def count(i, b, n):
                act.wait_ge(thr_ready, ROUNDS * (i - 1) + n + 1)
                act.activation(signs[:, :], mag[1 - b][:, :], ACT.Sign, bias=thr, scale=-1.0,
                               accum_out=bal).then_inc(counted, 1)

            def exps(j, t):
                act.wait_ge(max_ready[j], t + 1)
                act.activation(expd[:, :], scores[:, :], ACT.Exp, bias=neg_max, scale=unscale_r
                               ).then_inc(exp_ready[j], 1)

            def emit(i, b, like):
                cur, nxt, med, mid = parts(like)

                def median(n):
                    if med:
                        count(i, b, n)

                if mid:
                    for h in range(3):
                        w = min(4, IC - 4 * h)
                        act.wait_ge(vt_turned, 3 * (i - 2) + h + 1)
                        act.activation(vt_hi[:, 4 * h:4 * h + w, :],
                                       bank(2 + h, w * P).rearrange("p (c t) -> p c t", c=w),
                                       ACT.Copy).then_inc(vt_hi_ready, 1)
                median(0)
                if cur:
                    exps(1, i)
                median(1)
                if like == 0:
                    square(MB)
                    split_hi(MB)
                if cur:
                    pt_to_hi(1, i, 5)
                median(2)
                median(3)
                if mid:
                    xt_to_hi(3, i - 2)
                if like == 0:
                    square(MG)
                if cur:
                    xt_to_hi(2, i)
                if like == 0:
                    split_hi(MG)
                median(4)
                if mid:
                    exps(3, i - 2)
                median(5)
                median(6)
                if like == 0:
                    square(MU)
                if cur:
                    act.wait_ge(gate_done, i + 1)
                    if like >= 1:
                        act.wait_ge(val_ready, i)
                    act.activation(gate[:, :], bank(2, I), ACT.Tanh, scale=unscale_g
                                   ).then_inc(tanh_ready, 1)
                if like == 0:
                    split_hi(MU)
                if cur:
                    act.wait_ge(gate_ready, i + 1)
                    act.activation(mag[b][:, :], gate[:, :], ACT.Abs, accum_out=mag_sum
                                   ).then_inc(mag_ready, 1)
                if mid:
                    pt_to_hi(3, i - 2, 2)
                if nxt:
                    xt_to_hi(1, i + 1)
                if like == 0:
                    square(MD)
                    split_hi(MD)

            square(MR)
            square(MA)
            split_hi(MR)
            split_hi(MA)
            xt_to_hi(1, 0)
            loop_steps(act, emit)

        @block.vector
        def _(dve):
            link = Chain(dve, dve_chain)

            def make_scale(m):
                dve.wait_ge(norm_summed, pieces_before(m) + len(m.pieces))
                read = dve.tensor_reduce(norm2, bank(m.bank, m.width), AX.X, ALU.max)
                if m.bank == 1:
                    read.then_inc(out_read, 1)
                    dve.wait_ge(out_read, 1 if m is MB else 2)
                else:
                    link(read)
                link(dve.tensor_scalar(ints[:, 0:1], norm2.bitcast(I32), 23, None,
                                       ALU.logical_shift_right))
                link(dve.tensor_scalar(ints[:, 1:2], ints[:, 0:1], 1, None, ALU.add))
                link(dve.tensor_scalar(ints[:, 2:3], ints[:, 1:2], 1, None,
                                       ALU.logical_shift_right))
                link(dve.tensor_scalar(half_exp[m.name], ints[:, 2:3], 1.0, None, ALU.mult))
                link(dve.tensor_scalar(ints[:, 3:4], ints[:, 2:3], -1.0, 205.0, ALU.mult, ALU.add))
                dve.tensor_scalar(scale[m.name].bitcast(I32), ints[:, 3:4], 23, None,
                                  ALU.logical_shift_left).then_inc(scale_made, 1)
                dve.wait_ge(scale_made, MATS.index(m) + 1)

            def make_unscale(dst, names, plus):
                total_exp = half_exp[names[0]]
                for n in names[1:]:
                    link(dve.tensor_tensor(exp_sum, total_exp, half_exp[n], ALU.add))
                    total_exp = exp_sum
                link(dve.tensor_scalar(ints[:, 4:5], total_exp, float(plus), 0.0, ALU.add, ALU.max))
                link(dve.tensor_scalar(dst.bitcast(I32), ints[:, 4:5], 23, None,
                                       ALU.logical_shift_left))

            def split_lo(m):
                for n, (c, k, rows) in enumerate(m.pieces):
                    dve.wait_ge(w_hi_made, pieces_before(m) + n + 1)
                    dve.scalar_tensor_tensor(
                        out=lo[m.name][0:rows, c:c + k, :], in0=stage(m, c, k, rows),
                        scalar=scale[m.name][0:rows, :], in1=hi[m.name][0:rows, c:c + k, :],
                        op0=ALU.mult, op1=ALU.subtract).then_inc(w_lo_made, 1)
                dve.wait_ge(w_lo_made, pieces_before(m) + len(m.pieces))

            def norm_stats(j, src):
                link(dve.bn_stats(stats[j][:, :], src), wait_apart)
                dve.bn_aggr(mv[j][:, :], stats[j][:, :]).then_inc(var_ready[j], 1)

            def norm_apply(j, t, src):
                dve.wait_ge(rstd_ready[j], t + 1)
                dve.tensor_scalar(normed[j][:, :], src, mv[j][:, 0:1], rvar[j][:, 1:2],
                                  ALU.subtract, ALU.mult).then_inc(normed_ready[j], 1)

            def xt_to_lo(j, t):
                dve.wait_ge(xt_hi_ready[j], t + 1)
                dve.tensor_tensor(xt_lo[j][:, :, :], bank(0).rearrange("p (c t) -> p c t", c=DC),
                                  xt_hi[j][:, :, :], ALU.subtract).then_inc(xt_lo_ready[j], 1)

            def pt_to_lo(j, t, first):
                for h in range(2):
                    dve.wait_ge(pt_hi_ready[j], 2 * t + h + 1)
                    dve.tensor_tensor(pt_lo[:, 4 * h:4 * h + 4, :],
                                      bank(first + h).rearrange("p (c t) -> p c t", c=4),
                                      pt_hi[:, 4 * h:4 * h + 4, :],
                                      ALU.subtract).then_inc(pt_lo_ready[j], 1)

            def choose(j, t):
                dve.wait_ge(scores_done[j], t + 1)
                link(dve.tensor_copy(scores[:, :], bank(7, KE)), wait_apart)
                link(dve.max(top_a, scores[:, :]))
                dve.tensor_scalar(neg_max, top_a[:, 0:1], unscale_r, -1.0, ALU.mult, ALU.mult
                                  ).then_inc(max_ready[j], 1)
                link(dve.match_replace(out=work1[:, :], in_to_replace=top_a,
                                       in_values=scores[:, :], imm_value=NEG), wait_apart)
                link(dve.max(top_b, work1[:, :]), wait_apart)
                link(dve.match_replace(out=work2[:, :], in_to_replace=top_b,
                                       in_values=work1[:, :], imm_value=NEG))

            def route(j, t):
                dve.wait_ge(exp_ready[j], t + 1)
                link(dve.scalar_tensor_tensor(out=chosen[:, :], in0=work2[:, :], scalar=NEG / 2,
                                              in1=expd[:, :], op0=ALU.is_lt, op1=ALU.mult,
                                              accum_out=total))
                link(dve.reciprocal(inv_total, total))
                link(dve.tensor_scalar(weight[:, :], chosen[:, :], inv_total, GATE_S,
                                       ALU.mult, ALU.mult))
                dve.wait_ge(experts_done[j], t + 1)
                dve.tensor_tensor(
                    routed[:, :].rearrange("p (k r) -> p k r", r=RANK),
                    ps[:, 5 * BANK:5 * BANK + KR].rearrange("p (k r) -> p k r", r=RANK),
                    weight[:, :].unsqueeze(2).to_broadcast([P, KE, RANK]),
                    ALU.mult).then_inc(routed_ready[j], 1)

            def search(i, n):
                dve.wait_ge(counted, ROUNDS * (i - 1) + n + 1)
                link(dve.tensor_scalar(off, bal, -7.0, None, ALU.add))
                link(dve.tensor_scalar(far, off, off, 7.5 ** 2, ALU.mult, ALU.is_gt))
                link(dve.scalar_tensor_tensor(out=move, in0=off, scalar=far, in1=step,
                                              op0=ALU.mult, op1=ALU.mult))
                dve.scalar_tensor_tensor(out=thr, in0=move, scalar=DAMP[n], in1=thr,
                                         op0=ALU.mult, op1=ALU.add).then_inc(thr_ready, 1)

            def bisect(m):
                found, bit, trial, grown = (ints[:, c:c + 1] for c in (9, 10, 11, 12))
                dve.memset(found, 0)
                dve.memset(bit, 1 << 30)
                dve.drain()
                with dve.Fori(0, 31):
                    dve.tensor_tensor(trial, found, bit, ALU.bitwise_or)
                    dve.drain()
                    dve.tensor_scalar(keep[:, :], m, trial.bitcast(F32), None, ALU.is_lt, ALU.add,
                                      accum_out=above)
                    dve.drain()
                    dve.tensor_scalar(far, above, float(ZEROED) - 0.5, None, ALU.is_lt)
                    dve.drain()
                    dve.scalar_tensor_tensor(out=grown, in0=bit, scalar=far, in1=bit,
                                             op0=ALU.mult, op1=ALU.min)
                    dve.drain()
                    dve.tensor_tensor(found, found, grown, ALU.bitwise_or)
                    dve.tensor_scalar(bit, bit, 1, None, ALU.logical_shift_right)
                    dve.drain()
                exact = found.bitcast(F32)
                run = [cand.bitcast(F16)[:, h * I:(h + 1) * I] for h in range(2)]
                dve.tensor_scalar(keep[:, :], m, exact, None, ALU.is_lt, ALU.add, accum_out=above)
                dve.tensor_scalar(run[0], m, exact, None, ALU.is_equal)
                dve.drain()
                dve.tensor_scalar(off, above, -1.0, float(ZEROED), ALU.mult, ALU.add)
                s, src = 1, 0
                while s < I:
                    dve.tensor_tensor(run[1 - src][:, s:I], run[src][:, s:I], run[src][:, 0:I - s],
                                      ALU.add)
                    dve.tensor_copy(run[1 - src][:, 0:s], run[src][:, 0:s])
                    dve.drain()
                    s, src = 2 * s, 1 - src
                dve.tensor_scalar(run[1 - src], m, exact, None, ALU.is_equal)
                dve.drain()
                dve.scalar_tensor_tensor(out=run[src], in0=run[src], scalar=off, in1=run[1 - src],
                                         op0=ALU.is_gt, op1=ALU.mult)
                dve.drain()
                dve.scalar_tensor_tensor(out=keep[:, :], in0=m, scalar=exact, in1=run[src],
                                         op0=ALU.is_gt, op1=ALU.add)
                dve.drain()

            def select(i, b):
                m = mag[1 - b][:, :]
                dve.wait_ge(counted, ROUNDS * i)
                link(dve.scalar_tensor_tensor(out=cand, in0=m, scalar=thr, in1=m,
                                              op0=ALU.is_lt, op1=ALU.mult), wait_apart)
                link(dve.max(cand8, cand))
                link(dve.scalar_tensor_tensor(out=top_a, in0=evens, scalar=bal, in1=cand8,
                                              op0=ALU.is_equal, op1=ALU.mult, accum_out=kth))
                link(dve.tensor_scalar(keep[:, :], m, kth, None, ALU.is_gt, ALU.add,
                                       accum_out=above))
                link(dve.tensor_scalar(flags[:, 0:1], above, float(I - ZEROED), None,
                                       ALU.not_equal))
                link(dve.transpose(flags_t[:, :], flags[:, :]))
                link(dve.tensor_reduce(flagged, flags_t[:, :], AX.X, ALU.max), wait_apart)
                bad = [dve.value_load(flagged[q:q + 1, :], min_val=0, max_val=1)
                       for q in range(0, P, 32)]
                with dve.If(bad[0] + bad[1] + bad[2] + bad[3] != 0):
                    bisect(m)

            def emit(i, b, like):
                cur, nxt, med, mid = parts(like)

                def median(n):
                    if med:
                        search(i, n)

                if mid:
                    for h in range(3):
                        w = min(4, IC - 4 * h)
                        dve.wait_ge(vt_hi_ready, 3 * (i - 2) + h + 1)
                        dve.tensor_tensor(vt_lo[:, 4 * h:4 * h + w, :],
                                          bank(2 + h, w * P).rearrange("p (c t) -> p c t", c=w),
                                          vt_hi[:, 4 * h:4 * h + w, :],
                                          ALU.subtract).then_inc(vt_lo_ready, 1)
                median(0)
                if cur:
                    choose(1, i)
                    route(1, i)
                median(1)
                if like == 0:
                    make_scale(MB)
                    make_unscale(unscale_f, "ab", -24)
                    split_lo(MB)
                if cur:
                    pt_to_lo(1, i, 5)
                median(2)
                if mid:
                    dve.wait_ge(down_done, i - 1)
                    dve.scalar_tensor_tensor(out=x2[:, :], in0=bank(1), scalar=unscale_m,
                                             in1=x1[b][:, :], op0=ALU.mult, op1=ALU.add
                                             ).then_inc(out_read, 1)
                    dve.wait_ge(out_read, 2 * i - 1)
                    norm_stats(3, x2[:, :])
                median(3)
                if mid:
                    norm_apply(3, i - 2, x2[:, :])
                    xt_to_lo(3, i - 2)
                if cur:
                    dve.wait_ge(ffn1_done, i + 1)
                    dve.scalar_tensor_tensor(out=x1[b][:, :], in0=bank(4), scalar=unscale_f,
                                             in1=xin[b][:, :], op0=ALU.mult, op1=ALU.add
                                             ).then_inc(x1_ready, 1)
                    dve.wait_ge(x1_ready, i + 1)
                    norm_stats(2, x1[b][:, :])
                    norm_apply(2, i, x1[b][:, :])
                median(4)
                if like == 0:
                    make_scale(MG)
                    make_unscale(unscale_g, "g", 38)
                if cur:
                    xt_to_lo(2, i)
                if like == 0:
                    split_lo(MG)
                if mid:
                    choose(3, i - 2)
                    route(3, i - 2)
                median(5)
                if nxt:
                    dve.wait_ge(x_loaded[1 - b], nth(i + 1, 1 - b))
                    norm_stats(1, xin[1 - b][:, :])
                if med:
                    select(i, b)
                if nxt:
                    norm_apply(1, i + 1, xin[1 - b][:, :])
                if like == 0:
                    make_scale(MU)
                if cur:
                    dve.wait_ge(tanh_ready, i + 1)
                    dve.scalar_tensor_tensor(out=gate[:, :], in0=gate[:, :], scalar=1.0,
                                             in1=bank(2, I), op0=ALU.add, op1=ALU.mult
                                             ).then_inc(gate_ready, 1)
                if like == 0:
                    split_lo(MU)
                    for v in val:
                        link(dve.memset(v[:, I:IPAD], 0.0))
                if med:
                    dve.tensor_tensor(val[1 - b][:, 0:I], val[1 - b][:, 0:I], keep[:, :], ALU.mult
                                      ).then_inc(kept_ready, 1)
                if mid:
                    pt_to_lo(3, i - 2, 2)
                if cur:
                    dve.wait_ge(gate_ready, i + 1)
                    dve.wait_ge(up_done, i + 1)
                    dve.scalar_tensor_tensor(out=val[b][:, 0:I], in0=gate[:, :], scalar=VAL_S,
                                             in1=bank(5, I), op0=ALU.mult, op1=ALU.mult
                                             ).then_inc(val_ready, 1)
                    dve.wait_ge(mag_ready, i + 1)
                    link(dve.tensor_scalar(step, mag_sum, -SPACING / 2, None, ALU.mult))
                    dve.tensor_scalar(thr, mag_sum, GUESS, None, ALU.mult).then_inc(thr_ready, 1)
                if nxt:
                    xt_to_lo(1, i + 1)
                if like == 0:
                    make_scale(MD)
                    make_unscale(unscale_m, "gud", -83)
                    split_lo(MD)
                if mid:
                    dve.wait_ge(ffn3_done, i - 1)
                    if like >= 4:
                        dve.wait_ge(stored[b], nth(i - 4, b))
                    dve.scalar_tensor_tensor(out=y[b][:, :], in0=bank(1), scalar=unscale_f,
                                             in1=x2[:, :], op0=ALU.mult, op1=ALU.add
                                             ).then_inc(out_read, 1)

            link(dve.memset(flags[:, :], 0.0))
            for j in range(8):
                link(dve.memset(evens[:, j:j + 1], 2.0 * j))
            if LAST < P:
                link(dve.memset(hi["d"][LAST:P, IC - 1, :], 0.0))
                link(dve.memset(lo["d"][LAST:P, IC - 1, :], 0.0))
            dve.wait_ge(x_loaded[0], nth(0, 0))
            norm_stats(1, xin[0][:, :])
            norm_apply(1, 0, xin[0][:, :])
            make_scale(MR)
            make_unscale(unscale_r, "r", 39)
            make_scale(MA)
            split_lo(MR)
            split_lo(MA)
            xt_to_lo(1, 0)
            loop_steps(dve, emit, link, STEP_LINKS)


STEP_LINKS = 45


def kernel(**inputs):
    import numpy as np
    import concourse.bacc as bacc
    from concourse.bass_utils import run_bass_kernel_spmd

    x = np.ascontiguousarray(inputs["L0_attn_x"])
    B, S, D = x.shape
    a, b = inputs["L0_ffn_A"], inputs["L0_ffn_B"]
    K, R, _ = a.shape
    arrays = {
        "x": x.reshape(B * S, D),
        "w_r": np.ascontiguousarray(np.transpose(inputs["L0_ffn_Wr"])),
        "w_a": np.ascontiguousarray(np.transpose(np.reshape(a, (K * R, D)))),
        "w_b": np.ascontiguousarray(np.reshape(np.transpose(b, (0, 2, 1)), (K * R, D))),
        "w_g": np.ascontiguousarray(np.transpose(inputs["L0_attn_w_gate"])),
        "w_u": np.ascontiguousarray(np.transpose(inputs["L0_attn_w_up"])),
        "w_d": np.ascontiguousarray(np.transpose(inputs["L0_attn_w_down"])),
    }
    nc = bacc.Bacc("TRN2", target_bir_lowering=False, num_devices=1)
    args = [nc.dram_tensor(k, v.shape, mybir.dt.from_np(v.dtype), kind="ExternalInput").ap()
            for k, v in arrays.items()]
    args.append(nc.dram_tensor("out", (B * S, D), F32, kind="ExternalOutput").ap())
    build(nc, *args)
    r = run_bass_kernel_spmd(nc, [arrays], core_ids=[0])
    return np.reshape(r.results[0]["out"], (B, S, D))
```
